# Optimizing a Trainium2 kernel written in Bass

```python
import numpy as np
import jax
import jax.numpy as jnp

def _softmax(x, axis=-1):
    return jax.nn.softmax(x, axis=axis)

def _gelu(x):
    return jax.nn.gelu(x, approximate=True)

def _silu(x):
    return jax.nn.silu(x)

def _sigmoid(x):
    return jax.nn.sigmoid(x)

def _layernorm(x, axis=-1, eps=1e-05):
    m = jnp.mean(x, axis=axis, keepdims=True)
    v = jnp.var(x, axis=axis, keepdims=True)
    return (x - m) / jnp.sqrt(v + eps)

def _scatter_add(tgt, idx, src, axis=0):
    return tgt.at[idx].add(src)

def _segment_sum(src, seg, n):
    return jax.ops.segment_sum(src, seg, n)
kernel_name = 'mk_rec_standalone_d1_rec_r8_ae1014'

def setup_inputs(seed: int=0):
    np.random.seed(seed)
    _w = jnp.asarray

    def _rec_inputs():
        import jax
        import jax.numpy as jnp
        _rk = jax.random.key(seed)
        r_x0 = -0.000520686 + 1.00062 * jax.random.normal(jax.random.fold_in(_rk, 1), (2048, 32, 32), jnp.float32)
        return r_x0
    r_x0 = _rec_inputs()

    def _L0_rec_setup():
        import jax, jax.numpy as jnp
        import numpy as np
        B, M, D = (256, 32, 32)
        H1, H2 = (128, 64)

        def _cin_layer(x0, x, kernel):
            m = x0.shape[1]
            h_prev = x.shape[1]
            W = kernel.reshape(m, h_prev, kernel.shape[1])
            return jnp.einsum('bmd,bhd,mho->bod', x0, x, W)
        key = jax.random.key(seed)
        ks = jax.random.split(key, 5)
        x0 = jax.random.normal(ks[0], (B, M, D), dtype=jnp.float32)
        k1 = jax.random.normal(ks[1], (M * M, M), dtype=jnp.float32) * 0.05
        k2 = jax.random.normal(ks[2], (M * M, H1), dtype=jnp.float32) * 0.05
        k3 = jax.random.normal(ks[3], (M * H1, H2), dtype=jnp.float32) * 0.05
        kf = jax.random.normal(ks[4], (M + H1 + H2, 1), dtype=jnp.float32) * 0.05
        return {'x0': x0, 'k1': k1, 'k2': k2, 'k3': k3, 'kf': kf}
    _L0_rec_all = _L0_rec_setup()
    _L0_rec_in = {k: v for k, v in _L0_rec_all.items() if k in ('k1', 'k2', 'k3', 'kf')}
    del _L0_rec_all
    return {'r_x0': r_x0, 'L0_rec_k1': _L0_rec_in['k1'], 'L0_rec_k2': _L0_rec_in['k2'], 'L0_rec_k3': _L0_rec_in['k3'], 'L0_rec_kf': _L0_rec_in['kf']}

def reference(r_x0, L0_rec_k1, L0_rec_k2, L0_rec_k3, L0_rec_kf):
    import jax
    import jax.numpy as jnp

    def _L0_rec_ref(x0, k1, k2, k3, kf):
        import jax, jax.numpy as jnp
        import numpy as np
        B, M, D = (256, 32, 32)
        H1, H2 = (128, 64)

        def _cin_layer(x0, x, kernel):
            m = x0.shape[1]
            h_prev = x.shape[1]
            W = kernel.reshape(m, h_prev, kernel.shape[1])
            return jnp.einsum('bmd,bhd,mho->bod', x0, x, W)
        x = x0
        finals = []
        for k in (k1, k2, k3):
            x = _cin_layer(x0, x, k)
            finals.append(jnp.sum(x, axis=-1))
        finals = jnp.concatenate(finals, axis=-1)
        logit = finals @ kf
        return logit
    y = _L0_rec_ref(r_x0, L0_rec_k1, L0_rec_k2, L0_rec_k3, L0_rec_kf)
    return y

_drawn_inputs = setup_inputs


def setup_inputs(seed=0):
    import zlib

    import numpy as np

    out = dict(_drawn_inputs(seed))
    spreads = {}
    factors = {}
    for name, (base, spread) in spreads.items():
        noise = np.random.default_rng([zlib.crc32(name.encode()), seed]).standard_normal(out[name].shape)
        drawn = base * np.exp(spread * noise) if base else spread * noise
        out[name] = jnp.asarray(drawn.astype(out[name].dtype))
    for name, factor in factors.items():
        out[name] = (out[name] * factor).astype(out[name].dtype)
    return out
```

```python
from contextlib import ExitStack

import numpy as np

import concourse.bass as bass
from concourse import mybir

F32 = mybir.dt.float32
BF16 = mybir.dt.bfloat16
ALU = mybir.AluOpType
ACT = mybir.ActivationFunctionType
AX = mybir.AxisListType

B, M, D = 2048, 32, 32
H1, H2 = 128, 64
G = M
Q = 4
P = Q * M
BLOCK = 4096
BLOCKS = B * D // BLOCK
CHUNK = 512
HALF = BLOCK // 2
PAIRS = HALF // CHUNK
PAIR = 2 * CHUNK
QUARTER = BLOCK // Q
BCH = CHUNK // D
PARTS = 3
WRAP = 2 * M

SHIFTS = [(0, 0), (1, 2), (18, 4), (4, 4)]
ROWS = M + SHIFTS[1][0] + SHIFTS[1][1] * (Q - 1)
TILES = [(0, 1), (0, 2), (1, 2), (0, 3)]
SUM = 3


def shift(n, q):
    return SHIFTS[n][0] + SHIFTS[n][1] * q


def selections():
    r2 = np.zeros((PARTS, M, Q, M), np.float32)
    both = np.zeros((PARTS, M, Q, M), np.float32)
    for q in range(Q):
        for i in range(M):
            r2[:, (i + shift(2, q)) % M, q, i] += 1
            both[:, i, q, i] += 1
            both[:, (i + shift(3, q)) % M, q, i] += 1
    fold = both[0].reshape(M, P).T
    pick = np.stack([r2, both]).reshape(2, PARTS * M, P).transpose(1, 0, 2)
    return np.ascontiguousarray(pick), np.ascontiguousarray(np.concatenate([fold, fold], 1))


def wait(engine, semaphore, value):
    if not isinstance(value, int) or value > 0:
        engine.wait_ge(semaphore, value)


def cin_kernel(nc, x_blk, k1, k2t, k3t, kf, pick, fold, out, t_tab, t0_tab):
    with ExitStack() as ctx:
        def sb(name, shape, dt=F32):
            return ctx.enter_context(nc.sbuf_tensor(name, shape, dt))

        def pb(name, shape):
            return ctx.enter_context(nc.psum_tensor(name, shape, F32))

        def sem(name):
            return ctx.enter_context(nc.semaphore(name))

        r0 = [sb(f"r0_{u}", [P, BLOCK]) for u in range(2)]
        r1 = [sb(f"r1_{u}", [P, BLOCK]) for u in range(2)]
        x4 = [sb(f"x4_{u}", [P, QUARTER]) for u in range(2)]
        split = [sb(f"split_{u}", [P, PARTS, QUARTER], BF16) for u in range(2)]
        xs = [sb(f"xs_{u}", [PARTS * M, BLOCK], BF16) for u in range(2)]
        low = [sb(f"low_{u}", [P, QUARTER]) for u in range(2)]
        feat = [sb(f"feat_{u}", [P, HALF]) for u in range(2)]
        xy = [sb(f"xy_{u}", [3 * M, PAIRS * CHUNK]) for u in range(2)]
        prod = [sb(f"prod_{p}", [P, len(TILES), PAIR]) for p in range(2)]
        ysh = [sb(f"ysh_{p}", [3 * M, CHUNK]) for p in range(2)]
        k3s = r0[1][:, 0:M * H2].rearrange("h (m o) -> h m o", o=H2)
        k3kf = r1[1][:, 0:M * H2].rearrange("h (m o) -> h m o", o=H2)
        k2s = r1[1][:, M * H2:M * H2 + M * G]
        kf3b = sb("kf3b", [H1, H2])
        vk = sb("vk", [H1, M + 1])
        ts = sb("ts", [M + 1, M * G])
        wl = sb("wl", [P, len(TILES), 2 * G])
        wr = sb("wr", [P, len(TILES), 2 * G])
        w = sb("w", [P, len(TILES), 2 * G])
        wd = sb("wd", [2 * M, 2 * G])
        wf = sb("wf", [P, 4 * G])
        kf1 = sb("kf1", [P, 1])
        pick32 = sb("pick32", [PARTS * M, 2, P])
        picks = sb("picks", [PARTS * M, 2, P], BF16)
        folds = sb("folds", [P, 2 * M])
        ones = sb("ones", [3 * M, 1])
        tree = sb("tree", [3 * M, PAIRS * BCH, D // 2])
        sums = sb("sums", [3 * M, BLOCKS * PAIRS * BCH])
        result = sb("result", [1, BLOCKS, 2, PAIRS * BCH])

        rot = [pb(f"rot_{p}", [P, PAIR]) for p in range(2)]
        total = pb("total", [P, PAIR])
        acc = [pb(f"acc_{p}", [P, CHUNK]) for p in range(2)]

        k3_in, kf3_in, k2_in, kf2_in, kf1_in = (sem(n) for n in ("k3_in", "kf3_in", "k2_in", "kf2_in", "kf1_in"))
        consts_in, k1_in = sem("consts_in"), sem("k1_in")
        t_out, t_in = sem("t_out"), sem("t_in")
        r_in = [sem(f"r_in{u}") for u in range(2)]
        x4_in = [sem(f"x4_in{u}") for u in range(2)]
        xs_in = [sem(f"xs_in{u}") for u in range(2)]
        feat_in = [sem(f"feat_in{u}") for u in range(2)]
        stored = sem("stored")
        cleared, picks_ready, k3kf_ready, v_ready = sem("cleared"), sem("picks_ready"), sem("k3kf_ready"), sem("v_ready")
        t_ready, ts_ready, w_ready, fold_ready, wf_ready = (
            sem(n) for n in ("t_ready", "ts_ready", "w_ready", "fold_ready", "wf_ready"))
        w_summed = sem("w_summed")
        high_ready, low_ready, mid_ready, split_ready = (
            sem(n) for n in ("high_ready", "low_ready", "mid_ready", "split_ready"))
        rot_ready = sem("rot_ready")
        total_ready = sem("total_ready")
        products_ready = sem("products_ready")
        xs_free = sem("xs_free")
        squares_ready = sem("squares_ready")
        feat_ready = sem("feat_ready")
        acc_ready = sem("acc_ready")
        y_ready = sem("y_ready")
        xy_ready = sem("xy_ready")
        level = sem("level")
        sums_ready = sem("sums_ready")
        logits_ready, result_ready = sem("logits_ready"), sem("result_ready")

        LEVELS = 4

        block = ctx.enter_context(nc.Block())

        def x_rows(s, offset, pattern):
            return bass.AP(tensor=x_blk.tensor, offset=s * (ROWS * BLOCK) + offset, ap=pattern)

        def table(tab, left, right, quadrants):
            (a, da), (c, dc) = left, right
            return bass.AP(tensor=tab.tensor, offset=(a * WRAP + c) * G,
                           ap=[[(da * WRAP + dc) * G, quadrants], [(WRAP + 1) * G, M], [1, G]])

        def on_blocks(step):
            return step(0), step, step

        @block.sync
        def _(sp):
            def load_r(s, u):
                sp.dma_start(r0[u][:], x_rows(s, 0, [[0, Q], [BLOCK, M], [1, BLOCK]])).then_inc(r_in[u], 16)
                first, step = SHIFTS[1]
                sp.dma_start(r1[u][:], x_rows(s, first * BLOCK, [[step * BLOCK, Q], [BLOCK, M], [1, BLOCK]])
                             ).then_inc(r_in[u], 16)

            def load_feat(s, u):
                sp.dma_start(feat[u][2 * M:, :], x_rows(s, 0, [[HALF, 2], [BLOCK, M], [1, HALF]])
                             ).then_inc(feat_in[u], 16)

            def load_x4(s, u):
                sp.dma_start(x4[u][:], x_rows(s, 0, [[QUARTER, Q], [BLOCK, M], [1, QUARTER]])
                             ).then_inc(x4_in[u], 16)

            def place_parts(u):
                for part in range(PARTS):
                    for c in range(Q):
                        sp.dma_start(xs[u][part * M:(part + 1) * M, c * QUARTER:(c + 1) * QUARTER],
                                     split[u][c * M:(c + 1) * M, part, :]).then_inc(xs_in[u], 16)

            sp.dma_start(kf3b[:], bass.AP(tensor=kf.tensor, offset=M + H1, ap=[[0, H1], [1, H2]])).then_inc(kf3_in, 16)
            sp.dma_start(k3s, k3t).then_inc(k3_in, 16)
            sp.dma_start(vk[:, M:M + 1], kf[M:M + H1, :]).then_inc(kf2_in, 16)
            sp.dma_start(k2s, k2t).then_inc(k2_in, 16)
            load_x4(0, 0)
            load_x4(1, 1)
            load_r(0, 0)
            load_feat(0, 0)
            sp.wait_ge(split_ready, 1)
            sp.wait_ge(xs_free, 1)
            place_parts(0)
            load_x4(2, 0)

            def step(it, blocks=BLOCKS):
                for u in range(2):
                    k = 2 * it + u
                    nxt = (u + 1) % 2
                    inner = not isinstance(k, int)
                    if inner or k + 1 < blocks:
                        sp.wait_ge(split_ready, k + 2)
                        sp.wait_ge(xs_free, k + 2)
                        place_parts(nxt)
                    if inner or k + 3 < blocks:
                        load_x4(k + 3, nxt)
                    if inner or k + 1 < blocks:
                        if not inner and k == 0:
                            sp.wait_ge(t_ready, 2)
                        wait(sp, products_ready, 3 * PAIRS * k)
                        load_r(k + 1, nxt)
                        wait(sp, acc_ready, PAIRS * k)
                        load_feat(k + 1, nxt)

            step(0)
            with sp.Fori(1, BLOCKS // 2 - 2) as it:
                step(it)
            step(BLOCKS // 2 - 2)
            step(BLOCKS // 2 - 1)
            sp.wait_ge(result_ready, 4)
            sp.dma_start(out.rearrange("b one -> one b"),
                         result[:].rearrange("one s h n -> one (s h n)")).then_inc(stored, 16)
            sp.wait_ge(stored, 16)

        @block.scalar
        def _(act):
            act.dma_start(pick32[:], pick).then_inc(consts_in, 16)
            act.dma_start(folds[:], fold).then_inc(consts_in, 16)
            for half in range(2):
                act.dma_start(kf1[(2 * half + 1) * M:(2 * half + 2) * M, :], kf[0:M, :]).then_inc(kf1_in, 16)

            def high(u, n):
                act.wait_ge(x4_in[u], 16 * (n // 2 + 1) if isinstance(n, int) else n)
                nc.scalar.activation(split[u][:, 0, :], x4[u][:], ACT.Copy).then_inc(high_ready, 1)

            def mid(u):
                nc.scalar.activation(split[u][:, 1, :], low[u][:], ACT.Copy).then_inc(mid_ready, 1)

            for n in range(2):
                act.wait_ge(x4_in[n], 16)
                nc.scalar.activation(split[n][:, 0, :], x4[n][:], ACT.Copy).then_inc(high_ready, 1)
                act.wait_ge(low_ready, n + 1)
                mid(n)

            act.wait_ge(ts_ready, 2)
            for i in range(2):
                for j in range(2):
                    act.dma_start(t_tab[i * M:(i + 1) * M, j * M:(j + 1) * M, :],
                                  ts[0:M, :].rearrange("p (m g) -> p m g", g=G)).then_inc(t_out, 16)
            act.dma_start(t0_tab.rearrange("(one m) g -> one (m g)", one=1), ts[M:M + 1, :]).then_inc(t_out, 16)

            act.wait_ge(k1_in, 16 * 10)
            act.wait_ge(t_out, 16 * 5)
            for t, (left, right) in enumerate(TILES):
                short = t == SUM
                act.dma_start(wl[:, t, G:], table(t_tab, SHIFTS[left], SHIFTS[right], Q)).then_inc(t_in, 16)
                n = Q - 1 if short else Q
                act.dma_start(wr[0:n * M, t, G:], table(t_tab, SHIFTS[right], SHIFTS[left], n)).then_inc(t_in, 16)
            act.wait_ge(cleared, 2)
            for half in range(2):
                act.dma_start(wd[half * M:(half + 1) * M, G:], table(t_tab, (0, 0), (0, 0), 1)).then_inc(t_in, 16)
                act.dma_start(wf[(2 + half) * M:(3 + half) * M, (2 * half + 1) * G:(2 * half + 2) * G],
                              t0_tab).then_inc(t_in, 16)

            act.wait_ge(kf1_in, 32)

            def shift_y(g, p):
                act.wait_ge(acc_ready, g + 1)
                wait(act, xy_ready, g - 1)
                for half in range(2):
                    y = slice((2 * half + 1) * M, (2 * half + 2) * M)
                    x1 = slice(2 * half * M, (2 * half + 1) * M)
                    nc.scalar.activation(ysh[p][x1, :], acc[p][y, :], ACT.Identity, bias=kf1[y, :]
                                         ).then_inc(y_ready, 1)

            def step(it):
                for u in range(2):
                    k = 2 * it + u
                    for j in range(PAIRS):
                        g = PAIRS * k + j
                        p = j % 2
                        if j == 0:
                            act.wait_ge(feat_in[u], 16 * it + 16)
                            nc.scalar.activation(feat[u][0:2 * M, :], feat[u][2 * M:, :], ACT.Square
                                                 ).then_inc(feat_ready, 1)
                        act.wait_ge(total_ready, g + 1)
                        wait(act, acc_ready, g - 1)
                        nc.scalar.activation(prod[p][:, SUM, :], total[:], ACT.Square).then_inc(squares_ready, 1)
                        if not isinstance(g, int) or g >= 2:
                            shift_y(g - 2, p)
                        if not isinstance(k, int) or k + 2 < BLOCKS:
                            if j == 0:
                                act.wait_ge(x4_in[u], 16 * it + 32)
                                act.wait_ge(xs_in[u], 16 * PARTS * Q * (it + 1))
                                nc.scalar.activation(split[u][:, 0, :], x4[u][:], ACT.Copy).then_inc(high_ready, 1)
                            if j == 2:
                                act.wait_ge(low_ready, k + 3)
                                mid(u)

            step(0)
            with act.Fori(1, BLOCKS // 2 - 1) as it:
                step(it)
            step(BLOCKS // 2 - 1)
            for g in range(PAIRS * BLOCKS - 2, PAIRS * BLOCKS):
                shift_y(g, g % 2)

        @block.gpsimd
        def _(pool):
            pool.wait_ge(cleared, 2)
            for t, (left, right) in enumerate(TILES):
                pool.dma_start(wl[:, t, 0:G], table(k1, SHIFTS[left], SHIFTS[right], Q)).then_inc(k1_in, 16)
                n = Q - 1 if t == SUM else Q
                pool.dma_start(wr[0:n * M, t, 0:G], table(k1, SHIFTS[right], SHIFTS[left], n)).then_inc(k1_in, 16)
            for half in range(2):
                pool.dma_start(wd[half * M:(half + 1) * M, 0:G], table(k1, (0, 0), (0, 0), 1)).then_inc(k1_in, 16)

            def split_low(u, n):
                pool.wait_ge(high_ready, n)
                nc.gpsimd.tensor_tensor(low[u][:], x4[u][:], split[u][:, 0, :], ALU.subtract).then_inc(low_ready, 1)
                pool.wait_ge(mid_ready, n)
                nc.gpsimd.tensor_tensor(split[u][:, 2, :], low[u][:], split[u][:, 1, :], ALU.subtract
                                        ).then_inc(split_ready, 1)

            split_low(0, 1)
            split_low(1, 2)

            def sum_over_d(k, u):
                pool.wait_ge(xy_ready, PAIRS * k + PAIRS)
                src = xy[u][:].rearrange("p (b d) -> p b d", d=D)
                width = D // 2
                for n in range(LEVELS):
                    nc.gpsimd.tensor_tensor(tree[:, :, 0:width], src[:, :, 0:width], src[:, :, width:2 * width],
                                            ALU.add).then_inc(level, 1)
                    pool.wait_ge(level, LEVELS * k + n + 1)
                    src, width = tree, width // 2
                nc.gpsimd.tensor_tensor(sums[:, bass.ds(k * (PAIRS * BCH), PAIRS * BCH)], tree[:, :, 0], tree[:, :, 1],
                                        ALU.add).then_inc(sums_ready, 1)
                pool.wait_ge(sums_ready, k + 1)

            def step(it):
                for u in range(2):
                    k = 2 * it + u
                    if not isinstance(k, int) or k + 2 < BLOCKS:
                        split_low(u, k + 3)
                    if not isinstance(k, int) or k >= 1:
                        sum_over_d(k - 1, (u + 1) % 2)

            step(0)
            with pool.Fori(1, BLOCKS // 2 - 1) as it:
                step(it)
            step(BLOCKS // 2 - 1)
            sum_over_d(BLOCKS - 1, 1)

        @block.vector
        def _(dve):
            nc.vector.memset(wf[:], 0.0).then_inc(cleared, 1)
            nc.vector.memset(wr[(Q - 1) * M:, SUM, :], 0.0).then_inc(cleared, 1)
            nc.vector.memset(ones[:], 1.0).then_inc(xs_free, 2)
            for p in range(2):
                nc.vector.memset(ysh[p][M:2 * M, :], 0.0).then_inc(cleared, 1)
            dve.wait_ge(kf3_in, 16)
            dve.wait_ge(k3_in, 16)
            nc.vector.tensor_tensor(k3kf, k3s, kf3b[:].rearrange("h (one o) -> h one o", one=1)
                                    .to_broadcast([H1, M, H2]), ALU.mult).then_inc(k3kf_ready, 1)
            dve.wait_ge(k3kf_ready, 1)
            nc.vector.tensor_reduce(vk[:, 0:M], k3kf, AX.X, ALU.add).then_inc(v_ready, 1)
            dve.wait_ge(consts_in, 32)
            nc.vector.tensor_copy(picks[:], pick32[:]).then_inc(picks_ready, 1)
            for n in range(2):
                dve.wait_ge(t_ready, n + 1)
                nc.vector.tensor_copy(ts[:, n * CHUNK:(n + 1) * CHUNK], rot[0][0:M + 1, n * CHUNK:(n + 1) * CHUNK]
                                      ).then_inc(ts_ready, 1)

            def products(g, j, p, u):
                dve.wait_ge(rot_ready, g + 1)
                wait(dve, acc_ready, g - 1)

                def part(r):
                    return r[:].rearrange("q (half j c) -> q half j c", half=2, c=CHUNK)[:, :, j, :]

                def halves(a):
                    return a.rearrange("q (half c) -> q half c", half=2)

                nc.vector.tensor_tensor(halves(prod[p][:, 1, :]), halves(rot[p][:]), part(r0[u]), ALU.mult
                                        ).then_inc(products_ready, 1)
                nc.vector.tensor_tensor(halves(prod[p][:, 2, :]), halves(rot[p][:]), part(r1[u]), ALU.mult
                                        ).then_inc(products_ready, 1)
                nc.vector.tensor_tensor(halves(prod[p][:, 0, :]), part(r0[u]), part(r1[u]), ALU.mult
                                        ).then_inc(products_ready, 1)

            def multiply_xy(g, j, p, u):
                dve.wait_ge(y_ready, 2 * g + 2)
                nc.vector.tensor_tensor(xy[u][:, j * CHUNK:(j + 1) * CHUNK], acc[p][0:3 * M, :], ysh[p][:], ALU.mult
                                        ).then_inc(xy_ready, 1)

            def weights():
                dve.wait_ge(t_in, 16 * 12)
                dve.wait_ge(k1_in, 16 * 10)
                nc.vector.tensor_tensor(w[:, 0:SUM, :], wl[:, 0:SUM, :], wr[:, 0:SUM, :], ALU.add).then_inc(w_ready, 1)
                nc.vector.tensor_tensor(wl[:, SUM, :], wl[:, SUM, :], wr[:, SUM, :], ALU.add).then_inc(w_summed, 1)
                dve.wait_ge(w_summed, 1)
                nc.vector.tensor_scalar(w[:, SUM, :], wl[:, SUM, :], 0.5, None, ALU.mult).then_inc(w_ready, 1)
                dve.wait_ge(fold_ready, 1)
                for half in range(2):
                    rows = slice(half * M, (half + 1) * M)
                    nc.vector.tensor_tensor(wf[rows, 2 * half * G:(2 * half + 2) * G], wd[rows, :],
                                            acc[0][rows, 0:2 * G], ALU.subtract).then_inc(wf_ready, 1)

            def step(it):
                for u in range(2):
                    k = 2 * it + u
                    for j in range(PAIRS):
                        g = PAIRS * k + j
                        p = j % 2
                        if j == 0:
                            dve.wait_ge(r_in[u], 32 * it + 32)
                        products(g, j, p, u)
                        if isinstance(g, int) and g == 1:
                            weights()
                        if not isinstance(g, int) or g >= 2:
                            if j == 2:
                                wait(dve, sums_ready, k - 1)
                            multiply_xy(g - 2, (j - 2) % PAIRS, p, u if j >= 2 else (u + 1) % 2)

            step(0)
            with dve.Fori(1, BLOCKS // 2 - 1) as it:
                step(it)
            step(BLOCKS // 2 - 1)
            for g in range(PAIRS * BLOCKS - 2, PAIRS * BLOCKS):
                multiply_xy(g, g % PAIRS, g % 2, (BLOCKS - 1) % 2)
            dve.wait_ge(logits_ready, 4)
            for half in range(2):
                for n in range(2):
                    nc.vector.tensor_copy(
                        result[:, n * BLOCKS // 2:(n + 1) * BLOCKS // 2, half, :],
                        rot[half][0:1, n * CHUNK:(n + 1) * CHUNK].rearrange("one (s n) -> one s n", s=BLOCKS // 2)
                    ).then_inc(result_ready, 1)

        @block.tensor
        def _(pe):
            def chunks(j):
                return [slice(half * HALF + j * CHUNK, half * HALF + (j + 1) * CHUNK) for half in range(2)]

            def rotate(g, j, p, u, it):
                if j == 0:
                    pe.wait_ge(xs_in[u], 16 * PARTS * Q * (it + 1))
                wait(pe, products_ready, 3 * (g - 2) + 2)
                for half, c in enumerate(chunks(j)):
                    mm = nc.tensor.matmul(rot[p][:, half * CHUNK:(half + 1) * CHUNK], picks[:, 0, :], xs[u][:, c],
                                          start=True, stop=True)
                mm.then_inc(rot_ready, 1)
                wait(pe, squares_ready, g)
                for half, c in enumerate(chunks(j)):
                    mm = nc.tensor.matmul(total[:, half * CHUNK:(half + 1) * CHUNK], picks[:, 1, :], xs[u][:, c],
                                          start=True, stop=True)
                mm.then_inc(total_ready, 1)

            def contract(g, k, j, p, u):
                if j == 0:
                    pe.wait_ge(feat_ready, k + 1)
                wait(pe, xy_ready, g - 1)
                mm = nc.tensor.matmul(acc[p][:], wf[:], feat[u][:, j * CHUNK:(j + 1) * CHUNK], start=True,
                                      stop=False, skip_group_check=True)
                if j == PAIRS - 2:
                    mm.then_inc(xs_free, 1)
                for n, t in enumerate((1, 2, 0, SUM)):
                    if t == SUM:
                        pe.wait_ge(squares_ready, g + 1)
                    else:
                        pe.wait_ge(products_ready, 3 * g + n + 1)
                    for half in range(2):
                        mm = nc.tensor.matmul(acc[p][2 * half * M:(2 * half + 2) * M, :], w[:, t, :],
                                              prod[p][:, t, half * CHUNK:(half + 1) * CHUNK],
                                              start=False, stop=(t == SUM), skip_group_check=True)
                mm.then_inc(acc_ready, 1)

            pe.wait_ge(v_ready, 1)
            pe.wait_ge(kf2_in, 16)
            pe.wait_ge(k2_in, 16)
            for n in range(2):
                nc.tensor.matmul(rot[0][0:M + 1, n * CHUNK:(n + 1) * CHUNK], vk[:], k2s[:, n * CHUNK:(n + 1) * CHUNK],
                                 start=True, stop=True).then_inc(t_ready, 1)
            pe.wait_ge(picks_ready, 1)
            pe.wait_ge(ts_ready, 2)
            rotate(0, 0, 0, 0, 0)
            rotate(1, 1, 1, 0, 0)
            pe.wait_ge(w_ready, 2)
            nc.tensor.matmul(acc[0][0:2 * M, 0:2 * G], folds[:], w[:, SUM, :], start=True, stop=True
                             ).then_inc(fold_ready, 1)
            pe.wait_ge(wf_ready, 2)

            def step(it):
                for u in range(2):
                    k = 2 * it + u
                    for j in range(PAIRS):
                        g = PAIRS * k + j
                        nj, nu = (j + 1) % PAIRS, (u + (j + 1) // PAIRS) % 2
                        if not isinstance(g, int) or 0 < g and g + 1 < PAIRS * BLOCKS:
                            rotate(g + 1, nj, nj % 2, nu, it + (u + (j + 1) // PAIRS) // 2)
                        contract(g, k, j, j % 2, u)

            step(0)
            with pe.Fori(1, BLOCKS // 2 - 1) as it:
                step(it)
            step(BLOCKS // 2 - 1)
            pe.wait_ge(sums_ready, BLOCKS)
            for half in range(2):
                rows = slice(2 * half * M, (2 * half + 1) * M)
                for n in range(2):
                    nc.tensor.matmul(rot[half][0:1, n * CHUNK:(n + 1) * CHUNK], ones[rows, :],
                                     sums[rows, n * CHUNK:(n + 1) * CHUNK], start=True, stop=True
                                     ).then_inc(logits_ready, 1)


def kernel(r_x0, L0_rec_k1, L0_rec_k2, L0_rec_k3, L0_rec_kf):
    import concourse.bacc as bacc
    from concourse.bass_utils import run_bass_kernel_spmd

    x = np.asarray(r_x0).transpose(1, 0, 2).reshape(M, BLOCKS, BLOCK).transpose(1, 0, 2)
    k1 = np.asarray(L0_rec_k1).reshape(M, M, G)
    pick, fold = selections()
    arrays = {
        "x_blk": np.ascontiguousarray(np.concatenate([x, x[:, :ROWS - M]], axis=1)),
        "k1_tab": np.ascontiguousarray(np.tile(k1, (2, 2, 1))),
        "k2t": np.ascontiguousarray(np.asarray(L0_rec_k2).T),
        "k3t": np.ascontiguousarray(np.asarray(L0_rec_k3).reshape(M, H1, H2).transpose(1, 0, 2)),
        "kf": np.ascontiguousarray(L0_rec_kf),
        "pick": pick,
        "fold": fold,
    }
    nc = bacc.Bacc("TRN2", target_bir_lowering=False, num_devices=1)
    ins = [nc.dram_tensor(n, a.shape, mybir.dt.from_np(a.dtype), kind="ExternalInput").ap()
           for n, a in arrays.items()]
    out = nc.dram_tensor("logit", (B, 1), F32, kind="ExternalOutput").ap()
    t_tab = nc.dram_tensor("t_tab", (WRAP, WRAP, G), F32, kind="Internal").ap()
    t0_tab = nc.dram_tensor("t0_tab", (M, G), F32, kind="Internal").ap()
    cin_kernel(nc, *ins, out, t_tab, t0_tab)
    return run_bass_kernel_spmd(nc, [arrays], core_ids=[0]).results[0]["logit"]
```

```python
from contextlib import ExitStack

import numpy as np

import concourse.bass as bass
from concourse import mybir

F32 = mybir.dt.float32
BF16 = mybir.dt.bfloat16
ALU = mybir.AluOpType
ACT = mybir.ActivationFunctionType
AX = mybir.AxisListType

B, M, D = 2048, 32, 32
H1, H2 = 128, 64
G = M
Q = 4
P = Q * M
BLOCK = 4096
BLOCKS = B * D // BLOCK
CHUNK = 512
HALF = BLOCK // 2
PAIRS = HALF // CHUNK
PAIR = 2 * CHUNK
QUARTER = BLOCK // Q
BCH = CHUNK // D
PARTS = 3
WRAP = 2 * M

ZERO, A, B_, C = (0, 0), (9, 2), (6, 6), (7, 8)
ROWS = M + A[0] + A[1] * (Q - 1)
UV, UW, VW, WW = range(4)
TILES = 4
FIRST = {UV: (ZERO, A), UW: (ZERO, B_), VW: (A, C), WW: (B_, C)}
SECOND = {UW: (ZERO, C), VW: (A, B_)}
HALFWAY = slice((Q - 1) * M, P)


def index(pair, q, i):
    return tuple((i + first + step * q) % M for first, step in pair)


def rows_of_tables():
    orders = [[index(FIRST[t], q, i) for q in range(Q) for i in range(M)] for t in range(TILES)]
    rows = [[a * M + c for a, c in o] for o in orders] + [[c * M + a for a, c in o] for o in orders]
    return np.array(rows + [[(p % M) * (M + 1) for p in range(P)]])


def selections():
    pick = np.zeros((M, PARTS, Q, M), np.float32)
    fold = np.zeros((Q, M, 2, M), np.float32)
    home, fix = {}, np.zeros((P, 2, 2, P), np.float32)
    for q in range(Q):
        for i in range(M):
            for m in index((B_, C), q, i):
                pick[m, :, q, i] += 1
                fold[q, i, :, m] += 1
            for n, t in enumerate((UV, WW)):
                home[frozenset(index(FIRST[t], q, i))] = (n, q * M + i)
    for source, t in enumerate((UW, VW)):
        for q in range(Q):
            for i in range(M):
                n, row = home[frozenset(index(SECOND[t], q, i))]
                fix[q * M + i, n, source, row] += 1
    return (pick.reshape(PARTS * M, P),
            np.concatenate([fix.reshape(P, 4 * P), fold.reshape(P, 2 * M)], axis=1))


def wait(engine, semaphore, value):
    if not isinstance(value, int) or value > 0:
        engine.wait_ge(semaphore, value)


def cin_kernel(nc, x_blk, k1g, k2t, k3t, kf, pick, fixes, out, t_tab):
    with ExitStack() as ctx:
        def sb(name, shape, dt=F32):
            return ctx.enter_context(nc.sbuf_tensor(name, shape, dt))

        def pb(name, shape):
            return ctx.enter_context(nc.psum_tensor(name, shape, F32))

        def sem(name):
            return ctx.enter_context(nc.semaphore(name))

        r0 = [sb(f"r0_{u}", [P, BLOCK]) for u in range(2)]
        r1 = [sb(f"r1_{u}", [P, BLOCK]) for u in range(2)]
        x4 = [sb(f"x4_{u}", [P, QUARTER]) for u in range(2)]
        split = [sb(f"split_{u}", [P, PARTS, QUARTER], BF16) for u in range(2)]
        xs = [sb(f"xs_{u}", [M * PARTS, BLOCK], BF16) for u in range(2)]
        low = [sb(f"low_{u}", [P, QUARTER]) for u in range(2)]
        feat = [sb(f"feat_{u}", [P, HALF]) for u in range(2)]
        xy = [sb(f"xy_{u}", [3 * M, PAIRS * CHUNK]) for u in range(2)]
        prod = [sb(f"prod_{p}", [P, TILES, PAIR]) for p in range(2)]
        ysh = [sb(f"ysh_{p}", [3 * M, CHUNK]) for p in range(2)]
        k3s = r0[1][:, 0:M * H2].rearrange("h (m o) -> h m o", o=H2)
        k3kf = r1[1][:, 0:M * H2].rearrange("h (m o) -> h m o", o=H2)
        k2s = r1[1][:, M * H2:M * H2 + M * G]
        kf3b = sb("kf3b", [H1, H2])
        vk = sb("vk", [H1, M + 1])
        ts = sb("ts", [M + 1, 2, M * G])
        k1s = sb("k1s", [P, 2 * TILES + 1, G])
        tl = sb("tl", [P, TILES, G])
        tr = sb("tr", [P, TILES, G])
        td = sb("td", [P, G])
        w = sb("w", [P, TILES, 2 * G])
        wf = sb("wf", [P, 4 * G])
        kf1 = sb("kf1", [P, 1])
        pick32 = sb("pick32", [M * PARTS, P])
        picks = sb("picks", [M * PARTS, P], BF16)
        fixs = sb("fixs", [P, 4 * P + 2 * M])
        ones = sb("ones", [3 * M, 1])
        tree = sb("tree", [3 * M, PAIRS * BCH, D // 2])
        sums = sb("sums", [3 * M, BLOCKS * PAIRS * BCH])
        result = sb("result", [1, BLOCKS, 2, PAIRS * BCH])

        rot = [pb(f"rot_{p}", [P, PAIR]) for p in range(2)]
        acc = [pb(f"acc_{p}", [P, CHUNK]) for p in range(2)]
        logit = [pb(f"logit_{h}", [P, CHUNK]) for h in range(2)]
        fixes_ps = logit
        fold_ps = logit[0][0:2 * M, 2 * G:4 * G]

        kf3_in, k2_in, kf2_in, kf1_in = (sem(n) for n in ("kf3_in", "k2_in", "kf2_in", "kf1_in"))
        k3_in = [sem(f"k3_in{half}") for half in range(2)]
        pick_in, fix_in, k1_in = sem("pick_in"), sem("fix_in"), sem("k1_in")
        first_in = [sem(f"first_in{j}") for j in range(PAIRS)]
        t_out, t_in, t_last_in, td_in = (sem(n) for n in ("t_out", "t_in", "t_last_in", "td_in"))
        r_in = [sem(f"r_in{u}") for u in range(2)]
        x4_in = [sem(f"x4_in{u}") for u in range(2)]
        xs_in = [sem(f"xs_in{u}") for u in range(2)]
        feat_in = [sem(f"feat_in{u}") for u in range(2)]
        stored = sem("stored")
        cleared, picks_ready, k3kf_ready, v_ready = sem("cleared"), sem("picks_ready"), sem("k3kf_ready"), sem("v_ready")
        t_ready, ts_ready, w_ready, fix_ready, fixed, fold_ready, wf_ready = (
            sem(n) for n in ("t_ready", "ts_ready", "w_ready", "fix_ready", "fixed", "fold_ready", "wf_ready"))
        high_ready, low_ready, mid_ready, split_ready = (
            sem(n) for n in ("high_ready", "low_ready", "mid_ready", "split_ready"))
        rot_ready = sem("rot_ready")
        xs_free = sem("xs_free")
        squares_ready = sem("squares_ready")
        products_ready = sem("products_ready")
        feat_ready = sem("feat_ready")
        acc_ready = sem("acc_ready")
        y_ready = sem("y_ready")
        xy_ready = sem("xy_ready")
        level = sem("level")
        sums_ready = sem("sums_ready")
        last_sums, logits_ready, result_ready = sem("last_sums"), sem("logits_ready"), sem("result_ready")

        LEVELS = 4

        block = ctx.enter_context(nc.Block())

        def x_rows(s, offset, pattern):
            return bass.AP(tensor=x_blk.tensor, offset=s * (ROWS * BLOCK) + offset, ap=pattern)

        def table(left, right, quadrants=Q):
            (a, da), (c, dc) = left, right
            return bass.AP(tensor=t_tab.tensor, offset=(a * WRAP + c) * G,
                           ap=[[(da * WRAP + dc) * G, quadrants], [(WRAP + 1) * G, M], [1, G]])

        def part(r, j):
            return r[:].rearrange("q (half j c) -> q half j c", half=2, c=CHUNK)[:, :, j, :]

        LOGIT_PARTS = [(0, BLOCKS // 2), (BLOCKS // 2, BLOCKS - 1), (BLOCKS - 1, BLOCKS)]

        def logit_place(s):
            return M * (s // (BLOCKS // 2)), s % (BLOCKS // 2) * PAIRS * BCH

        T_READS = 16 * (2 * TILES - 2)
        POOL_T_READS = 16 * 2
        V_HALVES = [slice(0, M // 2), slice(M // 2, M)]

        @block.sync
        def _(sp):
            def load_r(s, u):
                sp.dma_start(r0[u][:], x_rows(s, 0, [[0, Q], [BLOCK, M], [1, BLOCK]])).then_inc(r_in[u], 16)
                sp.dma_start(r1[u][:], x_rows(s, A[0] * BLOCK, [[A[1] * BLOCK, Q], [BLOCK, M], [1, BLOCK]])
                             ).then_inc(r_in[u], 16)

            def load_first(j):
                for r, (first, step) in ((r0, ZERO), (r1, A)):
                    sp.dma_start(part(r[0], j),
                                 x_rows(0, first * BLOCK + j * CHUNK,
                                        [[step * BLOCK, Q], [BLOCK, M], [HALF, 2], [1, CHUNK]])).then_inc(first_in[j], 16)

            def load_feat(s, u):
                sp.dma_start(feat[u][2 * M:, :], x_rows(s, 0, [[HALF, 2], [BLOCK, M], [1, HALF]])
                             ).then_inc(feat_in[u], 16)

            def load_x4(s, u):
                sp.dma_start(x4[u][:], x_rows(s, 0, [[QUARTER, Q], [BLOCK, M], [1, QUARTER]])
                             ).then_inc(x4_in[u], 16)

            def place_parts(u):
                for c in range(Q):
                    sp.dma_start(xs[u][:, c * QUARTER:(c + 1) * QUARTER], split[u][c * M:(c + 1) * M, :, :]
                                 ).then_inc(xs_in[u], 16)

            sp.dma_start(kf3b[:], bass.AP(tensor=kf.tensor, offset=M + H1, ap=[[0, H1], [1, H2]])).then_inc(kf3_in, 16)
            for half in range(2):
                sp.dma_start(k3s[:, V_HALVES[half], :], k3t[:, V_HALVES[half], :]).then_inc(k3_in[half], 16)
            load_x4(0, 0)
            sp.dma_start(k2s, k2t).then_inc(k2_in, 16)
            load_x4(1, 1)
            load_first(0)
            load_first(1)
            sp.wait_ge(split_ready, 1)
            sp.wait_ge(xs_free, 1)
            place_parts(0)
            load_feat(0, 0)
            sp.wait_ge(t_out, 32)
            for t in (UW, VW, UV, WW):
                left, right = FIRST[t]
                sp.dma_start(tl[:, t, :], table(left, right)).then_inc(t_in, 16)
                if t in (UW, VW):
                    sp.dma_start(tr[:, t, :], table(right, left)).then_inc(t_in, 16)
            load_x4(2, 0)
            load_first(2)
            load_first(3)

            def step(it, blocks=BLOCKS):
                for u in range(2):
                    k = 2 * it + u
                    nxt = (u + 1) % 2
                    inner = not isinstance(k, int)
                    if inner or k + 1 < blocks:
                        sp.wait_ge(split_ready, k + 2)
                        sp.wait_ge(xs_free, k + 2)
                        place_parts(nxt)
                    if inner or k + 3 < blocks:
                        load_x4(k + 3, nxt)
                    if inner or k + 1 < blocks:
                        if not inner and k == 0:
                            sp.wait_ge(t_ready, 2)
                        wait(sp, products_ready, 3 * PAIRS * k)
                        load_r(k + 1, nxt)
                        wait(sp, acc_ready, PAIRS * k)
                        load_feat(k + 1, nxt)

            step(0)
            with sp.Fori(1, BLOCKS // 2 - 2) as it:
                step(it)
            step(BLOCKS // 2 - 2)
            step(BLOCKS // 2 - 1)
            flat_out, flat = out.rearrange("b one -> one b"), result[:].rearrange("one s h n -> one (s h n)")
            most = (BLOCKS - 1) * 2 * PAIRS * BCH
            sp.wait_ge(result_ready, 4)
            sp.dma_start(flat_out[:, 0:most], flat[:, 0:most]).then_inc(stored, 16)
            sp.wait_ge(result_ready, 6)
            sp.dma_start(flat_out[:, most:], flat[:, most:]).then_inc(stored, 16)
            sp.wait_ge(stored, 32)

        @block.scalar
        def _(act):
            act.dma_start(vk[:, M:M + 1], kf[M:M + H1, :]).then_inc(kf2_in, 16)
            act.dma_start(pick32[:], pick).then_inc(pick_in, 16)
            act.dma_start(fixs[:], fixes).then_inc(fix_in, 16)
            act.dma_start(k1s[:], k1g).then_inc(k1_in, 16)
            for half in range(2):
                act.dma_start(kf1[(2 * half + 1) * M:(2 * half + 2) * M, :], kf[0:M, :]).then_inc(kf1_in, 16)

            def high(u):
                nc.scalar.activation(split[u][:, 0, :], x4[u][:], ACT.Copy).then_inc(high_ready, 1)

            def mid(u):
                nc.scalar.activation(split[u][:, 1, :], low[u][:], ACT.Copy).then_inc(mid_ready, 1)

            act.wait_ge(x4_in[0], 16)
            high(0)
            act.wait_ge(low_ready, 1)
            mid(0)
            act.wait_ge(x4_in[1], 16)
            high(1)
            act.wait_ge(t_ready, 2)
            for copy in range(2):
                nc.scalar.copy(ts[:, copy, CHUNK:], rot[0][0:M + 1, CHUNK:]).then_inc(ts_ready, 1)

            act.wait_ge(ts_ready, 4)
            whole = t_tab.rearrange("p m g -> p (m g)")
            both = ts[:].rearrange("p copy n -> p (copy n)")
            act.dma_start(whole[0:M, :], both[0:M, :]).then_inc(t_out, 16)
            act.dma_start(whole[M:2 * M + 1, :], both).then_inc(t_out, 16)

            def shift_y(g, p):
                act.wait_ge(acc_ready, g + 1)
                wait(act, xy_ready, g - 1)
                for half in range(2):
                    y = slice((2 * half + 1) * M, (2 * half + 2) * M)
                    x1 = slice(2 * half * M, (2 * half + 1) * M)
                    nc.scalar.activation(ysh[p][x1, :], acc[p][y, :], ACT.Identity, bias=kf1[y, :]
                                         ).then_inc(y_ready, 1)

            def step(it):
                for u in range(2):
                    k = 2 * it + u
                    for j in range(PAIRS):
                        g = PAIRS * k + j
                        p = j % 2
                        act.wait_ge(rot_ready, g + 1)
                        wait(act, acc_ready, g - 1)
                        nc.scalar.activation(prod[p][:, WW, :], rot[p][:], ACT.Square).then_inc(squares_ready, 1)
                        if not isinstance(g, int) or g >= 2:
                            shift_y(g - 2, p)
                        early = isinstance(k, int) and k == 0
                        if early and j == 1:
                            act.wait_ge(low_ready, 2)
                            mid(1)
                            act.wait_ge(kf1_in, 32)
                        if j == (1 if early else 0):
                            act.wait_ge(feat_in[u], 16 * it + 16)
                            nc.scalar.activation(feat[u][0:2 * M, :], feat[u][2 * M:, :], ACT.Square
                                                 ).then_inc(feat_ready, 1)
                        if not isinstance(k, int) or k + 2 < BLOCKS:
                            if j == (1 if early else 0):
                                act.wait_ge(x4_in[u], 16 * it + 32)
                                act.wait_ge(xs_in[u], 16 * Q * (it + 1))
                                high(u)
                            if j == 2:
                                act.wait_ge(low_ready, k + 3)
                                mid(u)

            step(0)
            with act.Fori(1, BLOCKS // 2 - 1) as it:
                step(it)
            step(BLOCKS // 2 - 1)
            for g in range(PAIRS * BLOCKS - 2, PAIRS * BLOCKS):
                shift_y(g, g % 2)

        @block.gpsimd
        def _(pool):
            def split_low(u, n):
                pool.wait_ge(high_ready, n)
                nc.gpsimd.tensor_tensor(low[u][:], x4[u][:], split[u][:, 0, :], ALU.subtract).then_inc(low_ready, 1)
                pool.wait_ge(mid_ready, n)
                nc.gpsimd.tensor_tensor(split[u][:, 2, :], low[u][:], split[u][:, 1, :], ALU.subtract
                                        ).then_inc(split_ready, 1)

            split_low(0, 1)
            pool.wait_ge(t_out, 32)
            for t in (UV, WW):
                pool.dma_start(tr[:, t, :], table(*FIRST[t][::-1])).then_inc(t_last_in, 16)
            pool.dma_start(td[0:2 * M, :], bass.AP(tensor=t_tab.tensor, offset=0, ap=[[0, 2], [(WRAP + 1) * G, M], [1, G]])
                           ).then_inc(td_in, 16)
            pool.dma_start(td[2 * M:, :], bass.AP(tensor=t_tab.tensor, offset=2 * M * WRAP * G,
                                                  ap=[[0, 2], [G, M], [1, G]])).then_inc(td_in, 16)
            split_low(1, 2)

            def sum_over_d(k, u):
                pool.wait_ge(xy_ready, PAIRS * k + PAIRS)
                src = xy[u][:].rearrange("p (b d) -> p b d", d=D)
                width = D // 2
                for n in range(LEVELS):
                    nc.gpsimd.tensor_tensor(tree[:, :, 0:width], src[:, :, 0:width], src[:, :, width:2 * width],
                                            ALU.add).then_inc(level, 1)
                    pool.wait_ge(level, LEVELS * k + n + 1)
                    src, width = tree, width // 2
                nc.gpsimd.tensor_tensor(sums[:, bass.ds(k * (PAIRS * BCH), PAIRS * BCH)], tree[:, :, 0], tree[:, :, 1],
                                        ALU.add).then_inc(sums_ready, 1)
                pool.wait_ge(sums_ready, k + 1)

            def step(it):
                for u in range(2):
                    k = 2 * it + u
                    if not isinstance(k, int) or k + 2 < BLOCKS:
                        split_low(u, k + 3)
                    if not isinstance(k, int) or k >= 1:
                        sum_over_d(k - 1, (u + 1) % 2)

            step(0)
            with pool.Fori(1, BLOCKS // 2 - 1) as it:
                step(it)
            step(BLOCKS // 2 - 1)

        @block.vector
        def _(dve):
            nc.vector.memset(wf[:], 0.0).then_inc(cleared, 1)
            nc.vector.memset(ones[:], 1.0).then_inc(xs_free, 2)
            for p in range(2):
                nc.vector.memset(ysh[p][M:2 * M, :], 0.0).then_inc(cleared, 1)
            dve.wait_ge(kf3_in, 16)
            for half, ms in enumerate(V_HALVES):
                dve.wait_ge(k3_in[half], 16)
                nc.vector.tensor_tensor(k3kf[:, ms, :], k3s[:, ms, :], kf3b[:].rearrange("h (one o) -> h one o", one=1)
                                        .to_broadcast([H1, M // 2, H2]), ALU.mult).then_inc(k3kf_ready, 1)
                dve.wait_ge(k3kf_ready, half + 1)
                nc.vector.tensor_reduce(vk[:, ms], k3kf[:, ms, :], AX.X, ALU.add).then_inc(v_ready, 1)
            dve.wait_ge(pick_in, 16)
            nc.vector.tensor_copy(picks[:], pick32[:]).then_inc(picks_ready, 1)
            dve.wait_ge(t_ready, 1)
            for copy in range(2):
                nc.vector.tensor_copy(ts[:, copy, 0:CHUNK], rot[0][0:M + 1, 0:CHUNK]).then_inc(ts_ready, 1)

            def halves(a):
                return a.rearrange("q (half c) -> q half c", half=2)

            def multiply_uv(g, j, p, u):
                wait(dve, acc_ready, g - 1)

                nc.vector.tensor_tensor(halves(prod[p][:, UV, :]), part(r0[u], j), part(r1[u], j), ALU.mult
                                        ).then_inc(products_ready, 1)

            def multiply_w(g, j, p, u):
                dve.wait_ge(squares_ready, g + 1)
                nc.vector.tensor_tensor(halves(prod[p][:, UW, :]), halves(rot[p][:]), part(r0[u], j), ALU.mult
                                        ).then_inc(products_ready, 1)
                nc.vector.tensor_tensor(halves(prod[p][:, VW, :]), halves(rot[p][:]), part(r1[u], j), ALU.mult
                                        ).then_inc(products_ready, 1)

            def multiply_xy(g, j, p, u):
                dve.wait_ge(y_ready, 2 * g + 2)
                nc.vector.tensor_tensor(xy[u][:, j * CHUNK:(j + 1) * CHUNK], acc[p][0:3 * M, :], ysh[p][:], ALU.mult
                                        ).then_inc(xy_ready, 1)

            def sum_last(j):
                g = PAIRS * (BLOCKS - 1) + j
                at = g * BCH
                dve.wait_ge(xy_ready, g + 1)
                nc.vector.tensor_reduce(sums[:, at:at + BCH],
                                        xy[1][:, j * CHUNK:(j + 1) * CHUNK].rearrange("p (b d) -> p b d", d=D),
                                        AX.X, ALU.add).then_inc(last_sums, 1)

            def copy_logits(n):
                s0, s1 = LOGIT_PARTS[n]
                row, at = logit_place(s0)
                dve.wait_ge(logits_ready, 2 * n + 2)
                for half in range(2):
                    nc.vector.tensor_copy(
                        result[:, s0:s1, half, :],
                        logit[half][row:row + 1, at:at + (s1 - s0) * PAIRS * BCH].rearrange(
                            "one (s n) -> one s n", n=PAIRS * BCH)).then_inc(result_ready, 1)

            def weights():
                dve.wait_ge(k1_in, 16)
                nc.vector.tensor_tensor(w[:, :, 0:G], k1s[:, 0:TILES, :], k1s[:, TILES:2 * TILES, :], ALU.add
                                        ).then_inc(w_ready, 1)
                dve.wait_ge(t_in, T_READS)
                dve.wait_ge(t_last_in, POOL_T_READS)
                nc.vector.tensor_tensor(w[:, :, G:], tl[:], tr[:], ALU.add).then_inc(w_ready, 1)
                dve.wait_ge(w_ready, 2)
                nc.vector.tensor_copy(w[HALFWAY, VW, 0:G], k1s[HALFWAY, VW, :]).then_inc(w_ready, 1)
                nc.vector.tensor_copy(w[HALFWAY, VW, G:], tl[HALFWAY, VW, :]).then_inc(w_ready, 1)
                for n, t in enumerate((UV, WW)):
                    dve.wait_ge(fix_ready, n + 1)
                    nc.vector.tensor_tensor(w[:, t, :], w[:, t, :], fixes_ps[n][:, 0:2 * G], ALU.subtract
                                            ).then_inc(fixed, 1)
                dve.wait_ge(fixed, 2)
                nc.vector.tensor_scalar(w[:, WW, :], w[:, WW, :], 0.5, None, ALU.mult).then_inc(fixed, 1)
                dve.wait_ge(cleared, 1)
                dve.wait_ge(td_in, 32)
                for half in range(2):
                    rows = slice((2 + half) * M, (3 + half) * M)
                    nc.vector.tensor_copy(wf[rows, (2 * half + 1) * G:(2 * half + 2) * G], td[rows, :]
                                          ).then_inc(wf_ready, 1)
                dve.wait_ge(fold_ready, 1)
                for half in range(2):
                    rows = slice(half * M, (half + 1) * M)
                    for n, given in enumerate((k1s[rows, 2 * TILES, :], td[rows, :])):
                        nc.vector.tensor_tensor(wf[rows, (2 * half + n) * G:(2 * half + n + 1) * G], given,
                                                fold_ps[rows, n * G:(n + 1) * G], ALU.subtract).then_inc(wf_ready, 1)

            def step(it):
                for u in range(2):
                    k = 2 * it + u
                    for j in range(PAIRS):
                        g = PAIRS * k + j
                        p = j % 2
                        if not isinstance(g, int) or g != 1:
                            if isinstance(k, int) and k == 0:
                                dve.wait_ge(first_in[j], 32)
                            elif j == 0:
                                dve.wait_ge(r_in[u], 32 * it + 32 * u)
                            multiply_uv(g, j, p, u)
                        multiply_w(g, j, p, u)
                        if isinstance(g, int) and g == 0:
                            dve.wait_ge(first_in[1], 32)
                            multiply_uv(1, 1, 1, 0)
                            weights()
                        if not isinstance(g, int) or g >= 2:
                            if j == 2:
                                wait(dve, sums_ready, k - 1)
                            multiply_xy(g - 2, (j - 2) % PAIRS, p, u if j >= 2 else (u + 1) % 2)
                        if isinstance(k, int) and k == BLOCKS - 1 and j >= 2:
                            sum_last(j - 2)
                        if isinstance(k, int) and k == BLOCKS - 1 and j == 2:
                            copy_logits(0)

            step(0)
            with dve.Fori(1, BLOCKS // 2 - 1) as it:
                step(it)
            step(BLOCKS // 2 - 1)
            for j in range(PAIRS - 2, PAIRS):
                multiply_xy(PAIRS * (BLOCKS - 1) + j, j, j % 2, (BLOCKS - 1) % 2)
                sum_last(j)
                copy_logits(j - 1)

        @block.tensor
        def _(pe):
            def chunks(j):
                return [slice(half * HALF + j * CHUNK, half * HALF + (j + 1) * CHUNK) for half in range(2)]

            def rotate(g, j, p, u, it):
                if j == 0:
                    pe.wait_ge(xs_in[u], 16 * Q * (it + 1))
                wait(pe, products_ready, 3 * (g - 2) + 3)
                for half, c in enumerate(chunks(j)):
                    mm = nc.tensor.matmul(rot[p][:, half * CHUNK:(half + 1) * CHUNK], picks[:], xs[u][:, c],
                                          start=True, stop=True)
                mm.then_inc(rot_ready, 1)

            def contract(g, k, j, p, u):
                wait(pe, xy_ready, g - 1)
                for t in (UW, VW, UV, WW):
                    if t == WW:
                        pe.wait_ge(squares_ready, g + 1)
                    else:
                        pe.wait_ge(products_ready, 3 * g + t + 1)
                    for half in range(2):
                        mm = nc.tensor.matmul(acc[p][2 * half * M:(2 * half + 2) * M, :], w[:, t, :],
                                              prod[p][:, t, half * CHUNK:(half + 1) * CHUNK],
                                              start=(t == UW), stop=False, skip_group_check=True)
                    if t == UW and j == PAIRS - 2:
                        mm.then_inc(xs_free, 1)
                    if t == VW and isinstance(g, int) and g == 0:
                        pe.wait_ge(fixed, 3)
                        nc.tensor.matmul(fold_ps, fixs[:, 4 * P:], w[:, WW, :], start=True, stop=True
                                         ).then_inc(fold_ready, 1)
                if isinstance(g, int) and g == 0:
                    pe.wait_ge(wf_ready, 6)
                if j == 0:
                    pe.wait_ge(feat_ready, k + 1)
                nc.tensor.matmul(acc[p][:], wf[:], feat[u][:, j * CHUNK:(j + 1) * CHUNK], start=False,
                                 stop=True, skip_group_check=True).then_inc(acc_ready, 1)

            def logits(n):
                s0, s1 = LOGIT_PARTS[n]
                row, at = logit_place(s0)
                for half in range(2):
                    rows = slice(2 * half * M, (2 * half + 1) * M)
                    nc.tensor.matmul(logit[half][row:row + 1, at:at + (s1 - s0) * PAIRS * BCH], ones[rows, :],
                                     sums[rows, s0 * PAIRS * BCH:s1 * PAIRS * BCH], start=True, stop=True
                                     ).then_inc(logits_ready, 1)

            pe.wait_ge(v_ready, 2)
            pe.wait_ge(kf2_in, 16)
            pe.wait_ge(k2_in, 16)
            for n in range(2):
                nc.tensor.matmul(rot[0][0:M + 1, n * CHUNK:(n + 1) * CHUNK], vk[:], k2s[:, n * CHUNK:(n + 1) * CHUNK],
                                 start=True, stop=True).then_inc(t_ready, 1)
            pe.wait_ge(picks_ready, 1)
            pe.wait_ge(ts_ready, 4)
            rotate(0, 0, 0, 0, 0)
            rotate(1, 1, 1, 0, 0)
            pe.wait_ge(w_ready, 4)
            pe.wait_ge(fix_in, 16)
            for n in range(2):
                for source, t in enumerate((UW, VW)):
                    at = (2 * n + source) * P
                    mm = nc.tensor.matmul(fixes_ps[n][:, 0:2 * G], fixs[:, at:at + P], w[:, t, :],
                                          start=(source == 0), stop=(source == 1))
                mm.then_inc(fix_ready, 1)

            def step(it):
                for u in range(2):
                    k = 2 * it + u
                    for j in range(PAIRS):
                        g = PAIRS * k + j
                        nj, nu = (j + 1) % PAIRS, (u + (j + 1) // PAIRS) % 2
                        if not isinstance(g, int) or 0 < g and g + 1 < PAIRS * BLOCKS:
                            rotate(g + 1, nj, nj % 2, nu, it + (u + (j + 1) // PAIRS) // 2)
                        if isinstance(k, int) and k == BLOCKS - 1:
                            if j == 0:
                                pe.wait_ge(sums_ready, BLOCKS // 2)
                                logits(0)
                            if j == PAIRS - 1:
                                pe.wait_ge(sums_ready, BLOCKS - 1)
                                logits(1)
                        contract(g, k, j, j % 2, u)

            step(0)
            with pe.Fori(1, BLOCKS // 2 - 1) as it:
                step(it)
            step(BLOCKS // 2 - 1)
            pe.wait_ge(last_sums, PAIRS)
            logits(2)


def kernel(r_x0, L0_rec_k1, L0_rec_k2, L0_rec_k3, L0_rec_kf):
    import concourse.bacc as bacc
    from concourse.bass_utils import run_bass_kernel_spmd

    x = np.asarray(r_x0).transpose(1, 0, 2).reshape(M, BLOCKS, BLOCK).transpose(1, 0, 2)
    pick, fixes = selections()
    arrays = {
        "x_blk": np.ascontiguousarray(np.concatenate([x, x[:, :ROWS - M]], axis=1)),
        "k1g": np.ascontiguousarray(np.asarray(L0_rec_k1)[rows_of_tables()].transpose(1, 0, 2)),
        "k2t": np.ascontiguousarray(np.asarray(L0_rec_k2).T),
        "k3t": np.ascontiguousarray(np.asarray(L0_rec_k3).reshape(M, H1, H2).transpose(1, 0, 2)),
        "kf": np.ascontiguousarray(L0_rec_kf),
        "pick": pick,
        "fixes": fixes,
    }
    nc = bacc.Bacc("TRN2", target_bir_lowering=False, num_devices=1)
    ins = [nc.dram_tensor(n, a.shape, mybir.dt.from_np(a.dtype), kind="ExternalInput").ap()
           for n, a in arrays.items()]
    out = nc.dram_tensor("logit", (B, 1), F32, kind="ExternalOutput").ap()
    t_tab = nc.dram_tensor("t_tab", (WRAP + 1, WRAP, G), F32, kind="Internal").ap()
    cin_kernel(nc, *ins, out, t_tab)
    return run_bass_kernel_spmd(nc, [arrays], core_ids=[0]).results[0]["logit"]
```

```python
from contextlib import ExitStack

import numpy as np

import concourse.bass as bass
from concourse import mybir

F32 = mybir.dt.float32
BF16 = mybir.dt.bfloat16
ALU = mybir.AluOpType
ACT = mybir.ActivationFunctionType
AX = mybir.AxisListType

B, M, D = 2048, 32, 32
H1, H2 = 128, 64
G = M
Q = 4
P = Q * M
BLOCK = 4096
BLOCKS = B * D // BLOCK
CHUNK = 512
HALF = BLOCK // 2
PAIRS = HALF // CHUNK
PAIR = 2 * CHUNK
QUARTER = BLOCK // Q
BCH = CHUNK // D
PARTS = 3
WRAP = 2 * M

ZERO, A, B_, C = (0, 0), (9, 2), (6, 6), (7, 8)
ROWS = M + A[0] + A[1] * (Q - 1)
UV, UW, VW, WW = range(4)
TILES = 4
FIRST = {UV: (ZERO, A), UW: (ZERO, B_), VW: (A, C), WW: (B_, C)}
SECOND = {UW: (ZERO, C), VW: (A, B_)}
HALFWAY = slice((Q - 1) * M, P)


def index(pair, q, i):
    return tuple((i + first + step * q) % M for first, step in pair)


def rows_of_tables():
    orders = [[index(FIRST[t], q, i) for q in range(Q) for i in range(M)] for t in range(TILES)]
    rows = [[a * M + c for a, c in o] for o in orders] + [[c * M + a for a, c in o] for o in orders]
    return np.array(rows + [[(p % M) * (M + 1) for p in range(P)]])


def selections():
    pick = np.zeros((M, PARTS, Q, M), np.float32)
    fold = np.zeros((Q, M, 2, M), np.float32)
    home, fix = {}, np.zeros((P, 2, 2, P), np.float32)
    for q in range(Q):
        for i in range(M):
            for m in index((B_, C), q, i):
                pick[m, :, q, i] += 1
                fold[q, i, :, m] += 1
            for n, t in enumerate((UV, WW)):
                home[frozenset(index(FIRST[t], q, i))] = (n, q * M + i)
    for source, t in enumerate((UW, VW)):
        for q in range(Q):
            for i in range(M):
                n, row = home[frozenset(index(SECOND[t], q, i))]
                fix[q * M + i, n, source, row] += 1
    return (pick.reshape(PARTS * M, P),
            np.concatenate([fix.reshape(P, 4 * P), fold.reshape(P, 2 * M)], axis=1))


def wait(engine, semaphore, value):
    if not isinstance(value, int) or value > 0:
        engine.wait_ge(semaphore, value)


def cin_kernel(nc, x_blk, k1g, k2t, k3t, kf, pick, fixes, out, t_tab):
    with ExitStack() as ctx:
        def sb(name, shape, dt=F32):
            return ctx.enter_context(nc.sbuf_tensor(name, shape, dt))

        def pb(name, shape):
            return ctx.enter_context(nc.psum_tensor(name, shape, F32))

        def sem(name):
            return ctx.enter_context(nc.semaphore(name))

        r0 = [sb(f"r0_{u}", [P, BLOCK]) for u in range(2)]
        r1 = [sb(f"r1_{u}", [P, BLOCK]) for u in range(2)]
        x4 = [sb(f"x4_{u}", [P, QUARTER]) for u in range(2)]
        split = [sb(f"split_{u}", [P, PARTS, QUARTER], BF16) for u in range(2)]
        xs = [sb(f"xs_{u}", [M * PARTS, BLOCK], BF16) for u in range(2)]
        low = [sb(f"low_{u}", [P, QUARTER]) for u in range(2)]
        feat = [sb(f"feat_{u}", [P, HALF]) for u in range(2)]
        xy = [sb(f"xy_{u}", [3 * M, PAIRS * CHUNK]) for u in range(2)]
        prod = [sb(f"prod_{p}", [P, TILES, PAIR]) for p in range(2)]
        ysh = [sb(f"ysh_{p}", [3 * M, CHUNK]) for p in range(2)]
        k3s = r0[1][:, 0:M * H2].rearrange("h (m o) -> h m o", o=H2)
        k3kf = r1[1][:, 0:M * H2].rearrange("h (m o) -> h m o", o=H2)
        k2s = r1[1][:, M * H2:M * H2 + M * G]
        kf3b = sb("kf3b", [H1, H2])
        idle = split[1][:, 0, 0:CHUNK]
        vk = sb("vk", [H1, M + 1])
        ts = sb("ts", [M + 1, 2, M * G])
        k1s = sb("k1s", [P, 2 * TILES + 1, G])
        tl = sb("tl", [P, TILES, G])
        tr = sb("tr", [P, TILES, G])
        td = sb("td", [P, G])
        w = sb("w", [P, TILES, 2 * G])
        wf = sb("wf", [P, 4 * G])
        kf1 = sb("kf1", [P, 1])
        pick32 = sb("pick32", [M * PARTS, P])
        picks = sb("picks", [M * PARTS, P], BF16)
        fixs = sb("fixs", [P, 4 * P + 2 * M])
        ones = sb("ones", [3 * M, 2])
        tree = sb("tree", [3 * M, PAIRS * BCH, D // 2])
        sums = sb("sums", [3 * M, BLOCKS * PAIRS * BCH])
        result = sb("result", [2, BLOCKS * PAIRS * BCH])

        rot = [pb(f"rot_{p}", [P, PAIR]) for p in range(2)]
        acc = [pb(f"acc_{p}", [P, CHUNK]) for p in range(2)]
        last_banks = [pb(f"last_bank_{n}", [P, CHUNK]) for n in range(2)]
        fixes_ps = [bank[:, 0:2 * G] for bank in last_banks]
        fold_ps = last_banks[0][0:2 * M, 2 * G:4 * G]
        logit = last_banks[1]

        kf3_in, k2_in, kf2_in, kf1_in = (sem(n) for n in ("kf3_in", "k2_in", "kf2_in", "kf1_in"))
        k3_in = [sem(f"k3_in{half}") for half in range(2)]
        pick_in, fix_in, k1_in = sem("pick_in"), sem("fix_in"), sem("k1_in")
        pair_in = [[sem(f"pair_in{u}_{j}") for j in range(PAIRS)] for u in range(2)]
        t_out, t_first_in, t_vw_in, t_in, t_last_in, td_in = (
            sem(n) for n in ("t_out", "t_first_in", "t_vw_in", "t_in", "t_last_in", "td_in"))
        x4_in = [sem(f"x4_in{u}") for u in range(2)]
        xs_in = [sem(f"xs_in{u}") for u in range(2)]
        feat_in = [sem(f"feat_in{u}") for u in range(2)]
        stored = sem("stored")
        cleared, idle_ready, picks_ready = sem("cleared"), sem("idle_ready"), sem("picks_ready")
        k3kf_ready, k3kf_last, v_ready = sem("k3kf_ready"), sem("k3kf_last"), sem("v_ready")
        t_ready, ts_ready, w_ready, fix_ready, fixed, fold_ready, wf_ready = (
            sem(n) for n in ("t_ready", "ts_ready", "w_ready", "fix_ready", "fixed", "fold_ready", "wf_ready"))
        high_ready, low_ready, mid_ready, split_ready = (
            sem(n) for n in ("high_ready", "low_ready", "mid_ready", "split_ready"))
        rot_ready = sem("rot_ready")
        xs_free = sem("xs_free")
        squares_ready = sem("squares_ready")
        uv_ready = sem("uv_ready")
        products_ready = sem("products_ready")
        feat_ready = sem("feat_ready")
        acc_ready = sem("acc_ready")
        y_ready = sem("y_ready")
        xy_ready = sem("xy_ready")
        level = sem("level")
        sums_ready = sem("sums_ready")
        last_sums, logits_ready, result_ready = sem("last_sums"), sem("logits_ready"), sem("result_ready")

        LEVELS = 4

        block = ctx.enter_context(nc.Block())

        def x_rows(s, offset, pattern):
            return bass.AP(tensor=x_blk.tensor, offset=s * (ROWS * BLOCK) + offset, ap=pattern)

        def table(left, right):
            (a, da), (c, dc) = left, right
            return bass.AP(tensor=t_tab.tensor, offset=(a * WRAP + c) * G,
                           ap=[[(da * WRAP + dc) * G, Q], [(WRAP + 1) * G, M], [1, G]])

        def part(r, j):
            return r[:].rearrange("q (half j c) -> q half j c", half=2, c=CHUNK)[:, :, j, :]

        LOGIT_PARTS = [(0, BLOCKS // 2), (BLOCKS // 2, BLOCKS - 1), (BLOCKS - 1, BLOCKS)]

        def logit_place(s):
            return M * (s // (BLOCKS // 2)), s % (BLOCKS // 2) * PAIRS * BCH

        K3_HALVES = [slice(0, M // 2), slice(M // 2, M)]
        POOL_V = slice(3 * M // 4, M)

        @block.sync
        def _(sp):
            def load_pair(s, u, j):
                for r, (first, step) in ((r0, ZERO), (r1, A)):
                    sp.dma_start(part(r[u], j),
                                 x_rows(s, first * BLOCK + j * CHUNK,
                                        [[step * BLOCK, Q], [BLOCK, M], [HALF, 2], [1, CHUNK]])
                                 ).then_inc(pair_in[u][j], 16)

            def load_feat(s, u):
                sp.dma_start(feat[u][2 * M:, :], x_rows(s, 0, [[HALF, 2], [BLOCK, M], [1, HALF]])
                             ).then_inc(feat_in[u], 16)

            def load_x4(s, u):
                sp.dma_start(x4[u][:], x_rows(s, 0, [[QUARTER, Q], [BLOCK, M], [1, QUARTER]])
                             ).then_inc(x4_in[u], 16)

            def place_parts(u):
                for c in range(Q):
                    sp.dma_start(xs[u][:, c * QUARTER:(c + 1) * QUARTER], split[u][c * M:(c + 1) * M, :, :]
                                 ).then_inc(xs_in[u], 16)

            for half in range(2):
                sp.dma_start(k3s[:, K3_HALVES[half], :], k3t[:, K3_HALVES[half], :]).then_inc(k3_in[half], 16)
                if half == 0:
                    sp.dma_start(kf3b[:], bass.AP(tensor=kf.tensor, offset=M + H1, ap=[[0, H1], [1, H2]])
                                 ).then_inc(kf3_in, 16)
            sp.dma_start(k2s, k2t).then_inc(k2_in, 16)
            sp.dma_start(vk[:, M:M + 1], kf[M:M + H1, :]).then_inc(kf2_in, 16)
            load_x4(0, 0)
            sp.dma_start(pick32[:], pick).then_inc(pick_in, 16)
            load_pair(0, 0, 0)
            sp.dma_start(k1s[:], k1g).then_inc(k1_in, 16)
            sp.dma_start(fixs[:], fixes).then_inc(fix_in, 16)
            load_pair(0, 0, 1)
            sp.wait_ge(split_ready, 1)
            sp.wait_ge(xs_free, 1)
            place_parts(0)
            sp.wait_ge(t_out, 32)
            for t in (UW, VW):
                sp.dma_start(tl[:, t, :], table(*FIRST[t])).then_inc(t_first_in, 16)
            sp.dma_start(tr[:, UW, :], table(*FIRST[UW][::-1])).then_inc(t_first_in, 16)
            load_feat(0, 0)
            for t in (UV, WW):
                sp.dma_start(tl[:, t, :], table(*FIRST[t])).then_inc(t_in, 16)
            load_x4(1, 1)
            load_pair(0, 0, 2)
            for half in range(2):
                sp.dma_start(kf1[(2 * half + 1) * M:(2 * half + 2) * M, :], kf[0:M, :]).then_inc(kf1_in, 16)
            load_pair(0, 0, 3)
            sp.wait_ge(t_ready, 2)
            load_pair(1, 1, 0)
            sp.wait_ge(split_ready, 2)
            sp.wait_ge(xs_free, 2)
            place_parts(1)
            load_pair(1, 1, 1)
            load_feat(1, 1)
            load_x4(2, 0)
            load_pair(1, 1, 2)
            load_x4(3, 1)
            load_pair(1, 1, 3)

            def fetch(s, u, more=True):
                for j in range(PAIRS):
                    if j == PAIRS // 2:
                        sp.wait_ge(split_ready, s + 1)
                        sp.wait_ge(xs_free, s + 1)
                        place_parts(u)
                    if j == PAIRS - 1:
                        sp.wait_ge(acc_ready, PAIRS * (s - 1))
                        load_feat(s, u)
                    sp.wait_ge(products_ready, 2 * (PAIRS * (s - 2) + j + 1))
                    load_pair(s, u, j)
                if more:
                    load_x4(s + 2, u)

            with sp.Fori(1, BLOCKS // 2 - 1) as it:
                for u in range(2):
                    fetch(2 * it + u, u)
            for u in range(2):
                fetch(BLOCKS - 2 + u, u, more=False)
            for ready, (s0, s1) in ((2, (0, BLOCKS - 1)), (3, (BLOCKS - 1, BLOCKS))):
                sp.wait_ge(result_ready, ready)
                sp.dma_start(bass.AP(tensor=out.tensor, offset=s0 * 2 * PAIRS * BCH,
                                     ap=[[PAIRS * BCH, 2], [2 * PAIRS * BCH, s1 - s0], [1, PAIRS * BCH]]),
                             result[:, s0 * PAIRS * BCH:s1 * PAIRS * BCH].rearrange("h (s n) -> h s n", n=PAIRS * BCH)
                             ).then_inc(stored, 16)
            sp.wait_ge(stored, 32)

        @block.scalar
        def _(act):
            def high(u):
                nc.scalar.activation(split[u][:, 0, :], x4[u][:], ACT.Copy).then_inc(high_ready, 1)

            def mid(u):
                nc.scalar.activation(split[u][:, 1, :], low[u][:], ACT.Copy).then_inc(mid_ready, 1)

            act.wait_ge(x4_in[0], 16)
            high(0)
            act.wait_ge(t_ready, 2)
            for copy in range(2):
                nc.scalar.copy(ts[:, copy, CHUNK:], rot[0][0:M + 1, CHUNK:]).then_inc(ts_ready, 1)

            act.wait_ge(low_ready, 1)
            mid(0)

            act.wait_ge(ts_ready, 4)
            whole = t_tab.rearrange("p m g -> p (m g)")
            both = ts[:].rearrange("p copy n -> p (copy n)")
            act.dma_start(whole[0:M, :], both[0:M, :]).then_inc(t_out, 16)
            act.dma_start(whole[M:2 * M + 1, :], both).then_inc(t_out, 16)

            def square_x(it, u):
                act.wait_ge(feat_in[u], 16 * it + 16)
                nc.scalar.activation(feat[u][0:2 * M, :], feat[u][2 * M:, :], ACT.Square).then_inc(feat_ready, 1)

            def shift_y(g, p):
                act.wait_ge(acc_ready, g + 1)
                wait(act, xy_ready, g - 1)
                for half in range(2):
                    y = slice((2 * half + 1) * M, (2 * half + 2) * M)
                    x1 = slice(2 * half * M, (2 * half + 1) * M)
                    nc.scalar.activation(ysh[p][x1, :], acc[p][y, :], ACT.Identity, bias=kf1[y, :]
                                         ).then_inc(y_ready, 1)

            def step(it):
                for u in range(2):
                    k = 2 * it + u
                    for j in range(PAIRS):
                        g = PAIRS * k + j
                        p = j % 2
                        act.wait_ge(rot_ready, g + 1)
                        wait(act, acc_ready, g - 1)
                        nc.scalar.activation(prod[p][:, WW, :], rot[p][:], ACT.Square).then_inc(squares_ready, 1)
                        if not isinstance(g, int) or g >= 2:
                            shift_y(g - 2, p)
                        if isinstance(k, int) and k == 0:
                            if j == 1:
                                square_x(it, u)
                                act.wait_ge(x4_in[1], 16)
                                high(1)
                                act.wait_ge(low_ready, 2)
                                mid(1)
                                act.wait_ge(kf1_in, 32)
                            continue
                        if j == 0:
                            square_x(it, u)
                        if isinstance(k, int) and k == 1:
                            n = j // 2
                            if j % 2 == 0:
                                act.wait_ge(x4_in[n], 32)
                                act.wait_ge(xs_in[n], 16 * Q)
                                high(n)
                            else:
                                act.wait_ge(low_ready, 3 + n)
                                mid(n)
                        elif not isinstance(k, int) or k + 2 < BLOCKS:
                            if j == 1:
                                act.wait_ge(x4_in[u], 16 * it + 32)
                                act.wait_ge(xs_in[u], 16 * Q * (it + 1))
                                high(u)
                            if j == 2:
                                act.wait_ge(low_ready, k + 3)
                                mid(u)

            step(0)
            with act.Fori(1, BLOCKS // 2 - 1) as it:
                step(it)
            step(BLOCKS // 2 - 1)
            for g in range(PAIRS * BLOCKS - 2, PAIRS * BLOCKS):
                shift_y(g, g % 2)

        @block.gpsimd
        def _(pool):
            def split_low(u, n):
                pool.wait_ge(high_ready, n)
                nc.gpsimd.tensor_tensor(low[u][:], x4[u][:], split[u][:, 0, :], ALU.subtract).then_inc(low_ready, 1)
                pool.wait_ge(mid_ready, n)
                nc.gpsimd.tensor_tensor(split[u][:, 2, :], low[u][:], split[u][:, 1, :], ALU.subtract
                                        ).then_inc(split_ready, 1)

            pool.wait_ge(kf3_in, 16)
            pool.wait_ge(k3_in[1], 16)
            nc.gpsimd.tensor_tensor(k3kf[:, POOL_V, :], k3s[:, POOL_V, :],
                                    kf3b[:].rearrange("h (one o) -> h one o", one=1)
                                    .to_broadcast([H1, M // 4, H2]), ALU.mult).then_inc(k3kf_last, 1)
            pool.wait_ge(t_out, 32)
            pool.dma_start(tr[:, VW, :], table(*FIRST[VW][::-1])).then_inc(t_vw_in, 16)
            for t in (UV, WW):
                pool.dma_start(tr[:, t, :], table(*FIRST[t][::-1])).then_inc(t_last_in, 16)
            pool.dma_start(td[0:2 * M, :], bass.AP(tensor=t_tab.tensor, offset=0,
                                                   ap=[[0, 2], [(WRAP + 1) * G, M], [1, G]])).then_inc(td_in, 16)
            pool.dma_start(td[2 * M:, :], bass.AP(tensor=t_tab.tensor, offset=2 * M * WRAP * G,
                                                  ap=[[0, 2], [G, M], [1, G]])).then_inc(td_in, 16)
            split_low(1, 2)

            def sum_over_d(k, u):
                pool.wait_ge(xy_ready, PAIRS * k + PAIRS)
                src = xy[u][:].rearrange("p (b d) -> p b d", d=D)
                width = D // 2
                for n in range(LEVELS):
                    nc.gpsimd.tensor_tensor(tree[:, :, 0:width], src[:, :, 0:width], src[:, :, width:2 * width],
                                            ALU.add).then_inc(level, 1)
                    pool.wait_ge(level, LEVELS * k + n + 1)
                    src, width = tree, width // 2
                nc.gpsimd.tensor_tensor(sums[:, bass.ds(k * (PAIRS * BCH), PAIRS * BCH)], tree[:, :, 0], tree[:, :, 1],
                                        ALU.add).then_inc(sums_ready, 1)
                pool.wait_ge(sums_ready, k + 1)

            def step(it):
                for u in range(2):
                    k = 2 * it + u
                    if not isinstance(k, int) or k + 2 < BLOCKS:
                        split_low(u, k + 3)
                    if not isinstance(k, int) or k >= 1:
                        sum_over_d(k - 1, (u + 1) % 2)

            step(0)
            with pool.Fori(1, BLOCKS // 2 - 1) as it:
                step(it)
            step(BLOCKS // 2 - 1)

        @block.vector
        def _(dve):
            nc.vector.memset(idle, 0.0).then_inc(idle_ready, 1)
            nc.vector.memset(wf[:], 0.0).then_inc(cleared, 1)
            nc.vector.memset(ones[:], 0.0).then_inc(cleared, 1)
            for p in range(2):
                nc.vector.memset(ysh[p][M:2 * M, :], 0.0).then_inc(cleared, 1)
            dve.wait_ge(cleared, 2)
            for half in range(2):
                nc.vector.memset(ones[2 * half * M:(2 * half + 1) * M, half:half + 1], 1.0).then_inc(xs_free, 1)
            dve.wait_ge(kf3_in, 16)
            for n, ms in enumerate((K3_HALVES[0], slice(M // 2, POOL_V.start))):
                dve.wait_ge(k3_in[n], 16)
                nc.vector.tensor_tensor(k3kf[:, ms, :], k3s[:, ms, :], kf3b[:].rearrange("h (one o) -> h one o", one=1)
                                        .to_broadcast([H1, ms.stop - ms.start, H2]), ALU.mult).then_inc(k3kf_ready, 1)
                dve.wait_ge(k3kf_ready, n + 1)
                nc.vector.tensor_reduce(vk[:, ms], k3kf[:, ms, :], AX.X, ALU.add).then_inc(v_ready, 1)
            dve.wait_ge(k3kf_last, 1)
            nc.vector.tensor_reduce(vk[:, POOL_V], k3kf[:, POOL_V, :], AX.X, ALU.add).then_inc(v_ready, 1)
            dve.wait_ge(high_ready, 1)
            nc.vector.tensor_tensor(low[0][:], x4[0][:], split[0][:, 0, :], ALU.subtract).then_inc(low_ready, 1)
            dve.wait_ge(t_ready, 1)
            for copy in range(2):
                nc.vector.tensor_copy(ts[:, copy, 0:CHUNK], rot[0][0:M + 1, 0:CHUNK]).then_inc(ts_ready, 1)
            dve.wait_ge(mid_ready, 1)
            nc.vector.tensor_tensor(split[0][:, 2, :], low[0][:], split[0][:, 1, :], ALU.subtract
                                    ).then_inc(split_ready, 1)
            dve.wait_ge(pick_in, 16)
            nc.vector.tensor_copy(picks[:], pick32[:]).then_inc(picks_ready, 1)

            def halves(a):
                return a.rearrange("q (half c) -> q half c", half=2)

            def multiply_uv(g, j, p, u):
                wait(dve, acc_ready, g - 1)
                nc.vector.tensor_tensor(halves(prod[p][:, UV, :]), part(r0[u], j), part(r1[u], j), ALU.mult
                                        ).then_inc(uv_ready, 1)

            def multiply_w(g, j, p, u):
                dve.wait_ge(squares_ready, g + 1)
                nc.vector.tensor_tensor(halves(prod[p][:, UW, :]), halves(rot[p][:]), part(r0[u], j), ALU.mult
                                        ).then_inc(products_ready, 1)
                nc.vector.tensor_tensor(halves(prod[p][:, VW, :]), halves(rot[p][:]), part(r1[u], j), ALU.mult
                                        ).then_inc(products_ready, 1)

            def multiply_xy(g, j, p, u):
                dve.wait_ge(y_ready, 2 * g + 2)
                nc.vector.tensor_tensor(xy[u][:, j * CHUNK:(j + 1) * CHUNK], acc[p][0:3 * M, :], ysh[p][:], ALU.mult
                                        ).then_inc(xy_ready, 1)

            def sum_last(j):
                g = PAIRS * (BLOCKS - 1) + j
                at = g * BCH
                dve.wait_ge(xy_ready, g + 1)
                nc.vector.tensor_reduce(sums[:, at:at + BCH],
                                        xy[1][:, j * CHUNK:(j + 1) * CHUNK].rearrange("p (b d) -> p b d", d=D),
                                        AX.X, ALU.add).then_inc(last_sums, 1)

            def copy_logits(n):
                s0, s1 = LOGIT_PARTS[n]
                row, at = logit_place(s0)
                columns = (s1 - s0) * PAIRS * BCH
                dve.wait_ge(logits_ready, n + 1)
                nc.vector.tensor_copy(result[:, s0 * PAIRS * BCH:s1 * PAIRS * BCH], logit[row:row + 2, at:at + columns]
                                      ).then_inc(result_ready, 1)

            dve.wait_ge(pair_in[0][0], 32)
            multiply_uv(0, 0, 0, 0)
            dve.wait_ge(k1_in, 16)
            nc.vector.tensor_tensor(w[:, :, 0:G], k1s[:, 0:TILES, :], k1s[:, TILES:2 * TILES, :], ALU.add
                                    ).then_inc(w_ready, 1)
            dve.wait_ge(w_ready, 1)
            nc.vector.tensor_copy(w[HALFWAY, VW, 0:G], k1s[HALFWAY, VW, :]).then_inc(w_ready, 1)
            dve.wait_ge(pair_in[0][1], 32)
            multiply_uv(1, 1, 1, 0)
            dve.wait_ge(t_first_in, 16 * 3)
            dve.wait_ge(t_vw_in, 16)
            nc.vector.tensor_tensor(w[:, UW:VW + 1, G:], tl[:, UW:VW + 1, :], tr[:, UW:VW + 1, :], ALU.add
                                    ).then_inc(w_ready, 1)
            dve.wait_ge(w_ready, 3)
            nc.vector.tensor_copy(w[HALFWAY, VW, G:], tl[HALFWAY, VW, :]).then_inc(w_ready, 1)
            multiply_w(0, 0, 0, 0)
            dve.wait_ge(t_in, 16 * 2)
            dve.wait_ge(t_last_in, 16 * 2)
            for n, t in enumerate((UV, WW)):
                nc.vector.tensor_tensor(w[:, t, G:], tl[:, t, :], tr[:, t, :], ALU.add).then_inc(w_ready, 1)
            for n, t in enumerate((UV, WW)):
                dve.wait_ge(w_ready, 5 + n)
                dve.wait_ge(fix_ready, n + 1)
                nc.vector.tensor_tensor(w[:, t, :], w[:, t, :], fixes_ps[n], ALU.subtract
                                        ).then_inc(fixed, 1)
            dve.wait_ge(fixed, 2)
            nc.vector.tensor_scalar(w[:, WW, :], w[:, WW, :], 0.5, None, ALU.mult).then_inc(fixed, 1)
            dve.wait_ge(cleared, 1)
            dve.wait_ge(td_in, 32)
            for half in range(2):
                rows = slice((2 + half) * M, (3 + half) * M)
                nc.vector.tensor_copy(wf[rows, (2 * half + 1) * G:(2 * half + 2) * G], td[rows, :]
                                      ).then_inc(wf_ready, 1)
            dve.wait_ge(fold_ready, 1)
            for half in range(2):
                rows = slice(half * M, (half + 1) * M)
                for n, given in enumerate((k1s[rows, 2 * TILES, :], td[rows, :])):
                    nc.vector.tensor_tensor(wf[rows, (2 * half + n) * G:(2 * half + n + 1) * G], given,
                                            fold_ps[rows, n * G:(n + 1) * G], ALU.subtract).then_inc(wf_ready, 1)
            multiply_w(1, 1, 1, 0)

            def step(it):
                for u in range(2):
                    k = 2 * it + u
                    for j in range(PAIRS):
                        g = PAIRS * k + j
                        p = j % 2
                        if isinstance(g, int) and g < 2:
                            continue
                        dve.wait_ge(pair_in[u][j], 32 * (it + 1))
                        multiply_uv(g, j, p, u)
                        multiply_w(g, j, p, u)
                        if j == 2:
                            wait(dve, sums_ready, k - 1)
                        multiply_xy(g - 2, (j - 2) % PAIRS, p, u if j >= 2 else (u + 1) % 2)
                        if isinstance(k, int) and k == BLOCKS - 1 and j >= 2:
                            sum_last(j - 2)
                        if isinstance(k, int) and k == BLOCKS - 1 and j == 2:
                            copy_logits(0)

            step(0)
            with dve.Fori(1, BLOCKS // 2 - 1) as it:
                step(it)
            step(BLOCKS // 2 - 1)
            for j in range(PAIRS - 2, PAIRS):
                multiply_xy(PAIRS * (BLOCKS - 1) + j, j, j % 2, (BLOCKS - 1) % 2)
                sum_last(j)
                copy_logits(j - 1)

        @block.tensor
        def _(pe):
            def chunks(j):
                return [slice(half * HALF + j * CHUNK, half * HALF + (j + 1) * CHUNK) for half in range(2)]

            def rotate(g, j, p, u, it):
                if j == 0:
                    pe.wait_ge(xs_in[u], 16 * Q * (it + 1))
                wait(pe, products_ready, 2 * (g - 1))
                for half, c in enumerate(chunks(j)):
                    mm = nc.tensor.matmul(rot[p][:, half * CHUNK:(half + 1) * CHUNK], picks[:], xs[u][:, c],
                                          start=True, stop=True)
                mm.then_inc(rot_ready, 1)

            def contract(g, k, j, p, u):
                wait(pe, xy_ready, g - 1)
                order = (UW, VW, UV, WW)
                for t in order:
                    if t == WW:
                        pe.wait_ge(squares_ready, g + 1)
                    elif t == UV:
                        pe.wait_ge(uv_ready, g + 1)
                    else:
                        pe.wait_ge(products_ready, 2 * g + (1 if t == UW else 2))
                    for half in range(2):
                        mm = nc.tensor.matmul(acc[p][2 * half * M:(2 * half + 2) * M, :], w[:, t, :],
                                              prod[p][:, t, half * CHUNK:(half + 1) * CHUNK],
                                              start=(t == order[0]), stop=False, skip_group_check=True)
                    if t == order[0] and j == PAIRS - 2:
                        mm.then_inc(xs_free, 1)
                    if t == VW and isinstance(g, int) and g == 0:
                        pe.wait_ge(fixed, 3)
                        nc.tensor.matmul(fold_ps, fixs[:, 4 * P:], w[:, WW, :], start=True, stop=True
                                         ).then_inc(fold_ready, 1)
                if isinstance(g, int) and g == 0:
                    pe.wait_ge(wf_ready, 6)
                if j == 0:
                    pe.wait_ge(feat_ready, k + 1)
                nc.tensor.matmul(acc[p][:], wf[:], feat[u][:, j * CHUNK:(j + 1) * CHUNK], start=False,
                                 stop=True, skip_group_check=True).then_inc(acc_ready, 1)

            def logits(n):
                s0, s1 = LOGIT_PARTS[n]
                row, at = logit_place(s0)
                columns = (s1 - s0) * PAIRS * BCH
                nc.tensor.matmul(logit[row:row + 2, at:at + columns], ones[:],
                                 sums[:, s0 * PAIRS * BCH:s1 * PAIRS * BCH], start=True, stop=True
                                 ).then_inc(logits_ready, 1)

            def keep_clock_up(times):
                with pe.Fori(0, times):
                    for _ in range(4):
                        nc.tensor.matmul(acc[1][:], idle[:, 0:P], idle, start=True, stop=True)

            pe.wait_ge(idle_ready, 1)
            keep_clock_up(5)
            pe.wait_ge(v_ready, 3)
            pe.wait_ge(kf2_in, 16)
            pe.wait_ge(k2_in, 16)
            for n in range(2):
                nc.tensor.matmul(rot[0][0:M + 1, n * CHUNK:(n + 1) * CHUNK], vk[:], k2s[:, n * CHUNK:(n + 1) * CHUNK],
                                 start=True, stop=True).then_inc(t_ready, 1)
            keep_clock_up(9)
            pe.wait_ge(picks_ready, 1)
            pe.wait_ge(ts_ready, 4)
            rotate(0, 0, 0, 0, 0)
            rotate(1, 1, 1, 0, 0)
            pe.wait_ge(w_ready, 4)
            pe.wait_ge(fix_in, 16)
            for n in range(2):
                for source, t in enumerate((UW, VW)):
                    at = (2 * n + source) * P
                    mm = nc.tensor.matmul(fixes_ps[n], fixs[:, at:at + P], w[:, t, :],
                                          start=(source == 0), stop=(source == 1))
                mm.then_inc(fix_ready, 1)

            def step(it):
                for u in range(2):
                    k = 2 * it + u
                    for j in range(PAIRS):
                        g = PAIRS * k + j
                        nj, nu = (j + 1) % PAIRS, (u + (j + 1) // PAIRS) % 2
                        if not isinstance(g, int) or 0 < g and g + 1 < PAIRS * BLOCKS:
                            rotate(g + 1, nj, nj % 2, nu, it + (u + (j + 1) // PAIRS) // 2)
                        if isinstance(k, int) and k == BLOCKS - 1 and j == 0:
                            pe.wait_ge(sums_ready, BLOCKS // 2)
                            logits(0)
                        contract(g, k, j, j % 2, u)

            step(0)
            with pe.Fori(1, BLOCKS // 2 - 1) as it:
                step(it)
            step(BLOCKS // 2 - 1)
            pe.wait_ge(sums_ready, BLOCKS - 1)
            logits(1)
            pe.wait_ge(last_sums, PAIRS)
            logits(2)


def kernel(r_x0, L0_rec_k1, L0_rec_k2, L0_rec_k3, L0_rec_kf):
    import concourse.bacc as bacc
    from concourse.bass_utils import run_bass_kernel_spmd

    x = np.asarray(r_x0).transpose(1, 0, 2).reshape(M, BLOCKS, BLOCK).transpose(1, 0, 2)
    pick, fixes = selections()
    arrays = {
        "x_blk": np.ascontiguousarray(np.concatenate([x, x[:, :ROWS - M]], axis=1)),
        "k1g": np.ascontiguousarray(np.asarray(L0_rec_k1)[rows_of_tables()].transpose(1, 0, 2)),
        "k2t": np.ascontiguousarray(np.asarray(L0_rec_k2).T),
        "k3t": np.ascontiguousarray(np.asarray(L0_rec_k3).reshape(M, H1, H2).transpose(1, 0, 2)),
        "kf": np.ascontiguousarray(L0_rec_kf),
        "pick": pick,
        "fixes": fixes,
    }
    nc = bacc.Bacc("TRN2", target_bir_lowering=False, num_devices=1)
    ins = [nc.dram_tensor(n, a.shape, mybir.dt.from_np(a.dtype), kind="ExternalInput").ap()
           for n, a in arrays.items()]
    out = nc.dram_tensor("logit", (B, 1), F32, kind="ExternalOutput").ap()
    t_tab = nc.dram_tensor("t_tab", (WRAP + 1, WRAP, G), F32, kind="Internal").ap()
    cin_kernel(nc, *ins, out, t_tab)
    return run_bass_kernel_spmd(nc, [arrays], core_ids=[0]).results[0]["logit"]
```
